# Optimizing a Trainium2 kernel written in Bass

```python
import numpy as np
import jax
import jax.numpy as jnp

def _softmax(x, axis=-1):
    return jax.nn.softmax(x, axis=axis)

def _gelu(x):
    return jax.nn.gelu(x, approximate=True)

def _silu(x):
    return jax.nn.silu(x)

def _sigmoid(x):
    return jax.nn.sigmoid(x)

def _layernorm(x, axis=-1, eps=1e-05):
    m = jnp.mean(x, axis=axis, keepdims=True)
    v = jnp.var(x, axis=axis, keepdims=True)
    return (x - m) / jnp.sqrt(v + eps)

def _scatter_add(tgt, idx, src, axis=0):
    return tgt.at[idx].add(src)

def _segment_sum(src, seg, n):
    return jax.ops.segment_sum(src, seg, n)
kernel_name = 'mk_dlrm_tower_d1_rec_r8_a22263'

def setup_inputs(seed: int=0):
    np.random.seed(seed)
    _w = jnp.asarray

    def _rec_inputs():
        import jax
        import jax.numpy as jnp
        _tk = jax.random.key(seed)
        ids = jnp.stack([jax.random.randint(jax.random.fold_in(_tk, 200 + f), (512,), 0, v, jnp.int32) for f, v in enumerate([1250, 1000, 1250, 125000, 12500, 1000, 12500, 12500, 1250, 1250, 1250, 1000, 12500, 1250, 12500, 1250, 1000, 1000, 1250, 12500, 12500, 12500, 1000, 1250, 1000, 1000])], axis=1)
        tbl_0 = 0.05 * jax.random.normal(jax.random.fold_in(_tk, 500 + 0), (1250, 128), jnp.float32)
        tbl_1 = 0.05 * jax.random.normal(jax.random.fold_in(_tk, 500 + 1), (1000, 128), jnp.float32)
        tbl_2 = 0.05 * jax.random.normal(jax.random.fold_in(_tk, 500 + 2), (1250, 128), jnp.float32)
        tbl_3 = 0.05 * jax.random.normal(jax.random.fold_in(_tk, 500 + 3), (125000, 128), jnp.float32)
        tbl_4 = 0.05 * jax.random.normal(jax.random.fold_in(_tk, 500 + 4), (12500, 128), jnp.float32)
        tbl_5 = 0.05 * jax.random.normal(jax.random.fold_in(_tk, 500 + 5), (1000, 128), jnp.float32)
        tbl_6 = 0.05 * jax.random.normal(jax.random.fold_in(_tk, 500 + 6), (12500, 128), jnp.float32)
        tbl_7 = 0.05 * jax.random.normal(jax.random.fold_in(_tk, 500 + 7), (12500, 128), jnp.float32)
        tbl_8 = 0.05 * jax.random.normal(jax.random.fold_in(_tk, 500 + 8), (1250, 128), jnp.float32)
        tbl_9 = 0.05 * jax.random.normal(jax.random.fold_in(_tk, 500 + 9), (1250, 128), jnp.float32)
        tbl_10 = 0.05 * jax.random.normal(jax.random.fold_in(_tk, 500 + 10), (1250, 128), jnp.float32)
        tbl_11 = 0.05 * jax.random.normal(jax.random.fold_in(_tk, 500 + 11), (1000, 128), jnp.float32)
        tbl_12 = 0.05 * jax.random.normal(jax.random.fold_in(_tk, 500 + 12), (12500, 128), jnp.float32)
        tbl_13 = 0.05 * jax.random.normal(jax.random.fold_in(_tk, 500 + 13), (1250, 128), jnp.float32)
        tbl_14 = 0.05 * jax.random.normal(jax.random.fold_in(_tk, 500 + 14), (12500, 128), jnp.float32)
        tbl_15 = 0.05 * jax.random.normal(jax.random.fold_in(_tk, 500 + 15), (1250, 128), jnp.float32)
        tbl_16 = 0.05 * jax.random.normal(jax.random.fold_in(_tk, 500 + 16), (1000, 128), jnp.float32)
        tbl_17 = 0.05 * jax.random.normal(jax.random.fold_in(_tk, 500 + 17), (1000, 128), jnp.float32)
        tbl_18 = 0.05 * jax.random.normal(jax.random.fold_in(_tk, 500 + 18), (1250, 128), jnp.float32)
        tbl_19 = 0.05 * jax.random.normal(jax.random.fold_in(_tk, 500 + 19), (12500, 128), jnp.float32)
        tbl_20 = 0.05 * jax.random.normal(jax.random.fold_in(_tk, 500 + 20), (12500, 128), jnp.float32)
        tbl_21 = 0.05 * jax.random.normal(jax.random.fold_in(_tk, 500 + 21), (12500, 128), jnp.float32)
        tbl_22 = 0.05 * jax.random.normal(jax.random.fold_in(_tk, 500 + 22), (1000, 128), jnp.float32)
        tbl_23 = 0.05 * jax.random.normal(jax.random.fold_in(_tk, 500 + 23), (1250, 128), jnp.float32)
        tbl_24 = 0.05 * jax.random.normal(jax.random.fold_in(_tk, 500 + 24), (1000, 128), jnp.float32)
        tbl_25 = 0.05 * jax.random.normal(jax.random.fold_in(_tk, 500 + 25), (1000, 128), jnp.float32)
        _rk = jax.random.fold_in(_tk, 7)
        r_dense_features = -0.000520686 + 1.00062 * jax.random.normal(jax.random.fold_in(_rk, 101), (512, 128), jnp.float32)
        W_top1 = 0.0405887 * jax.random.normal(jax.random.fold_in(_tk, 801), (607, 512), jnp.float32)
        W_top2 = 0.0441942 * jax.random.normal(jax.random.fold_in(_tk, 802), (512, 256), jnp.float32)
        W_top3 = 0.0625 * jax.random.normal(jax.random.fold_in(_tk, 803), (256, 1), jnp.float32)
        b_top1 = jnp.zeros((512,), jnp.float32)
        b_top2 = jnp.zeros((256,), jnp.float32)
        return (r_dense_features, ids, tbl_0, tbl_1, tbl_2, tbl_3, tbl_4, tbl_5, tbl_6, tbl_7, tbl_8, tbl_9, tbl_10, tbl_11, tbl_12, tbl_13, tbl_14, tbl_15, tbl_16, tbl_17, tbl_18, tbl_19, tbl_20, tbl_21, tbl_22, tbl_23, tbl_24, tbl_25, W_top1, b_top1, W_top2, b_top2, W_top3)
    r_dense_features, ids, tbl_0, tbl_1, tbl_2, tbl_3, tbl_4, tbl_5, tbl_6, tbl_7, tbl_8, tbl_9, tbl_10, tbl_11, tbl_12, tbl_13, tbl_14, tbl_15, tbl_16, tbl_17, tbl_18, tbl_19, tbl_20, tbl_21, tbl_22, tbl_23, tbl_24, tbl_25, W_top1, b_top1, W_top2, b_top2, W_top3 = _rec_inputs()

    def _L0_rec_setup():
        import jax, jax.numpy as jnp
        import numpy as np
        F = 26
        N = F + 1
        _TRIU_I, _TRIU_J = np.triu_indices(N, k=1)
        key = jax.random.key(seed)
        k1, k2 = jax.random.split(key)
        B, D = (2048, 128)
        dense_features = jax.random.normal(k1, (B, D), dtype=jnp.float32)
        sparse_features = jax.random.normal(k2, (B, F, D), dtype=jnp.float32)
        return {'dense_features': dense_features, 'sparse_features': sparse_features}
    _L0_rec_all = _L0_rec_setup()
    _L0_rec_in = {k: v for k, v in _L0_rec_all.items() if k in ()}
    del _L0_rec_all
    return {'r_dense_features': r_dense_features, 'ids': ids, 'tbl_0': tbl_0, 'tbl_1': tbl_1, 'tbl_2': tbl_2, 'tbl_3': tbl_3, 'tbl_4': tbl_4, 'tbl_5': tbl_5, 'tbl_6': tbl_6, 'tbl_7': tbl_7, 'tbl_8': tbl_8, 'tbl_9': tbl_9, 'tbl_10': tbl_10, 'tbl_11': tbl_11, 'tbl_12': tbl_12, 'tbl_13': tbl_13, 'tbl_14': tbl_14, 'tbl_15': tbl_15, 'tbl_16': tbl_16, 'tbl_17': tbl_17, 'tbl_18': tbl_18, 'tbl_19': tbl_19, 'tbl_20': tbl_20, 'tbl_21': tbl_21, 'tbl_22': tbl_22, 'tbl_23': tbl_23, 'tbl_24': tbl_24, 'tbl_25': tbl_25, 'W_top1': W_top1, 'b_top1': b_top1, 'W_top2': W_top2, 'b_top2': b_top2, 'W_top3': W_top3}

def reference(r_dense_features, ids, tbl_0, tbl_1, tbl_2, tbl_3, tbl_4, tbl_5, tbl_6, tbl_7, tbl_8, tbl_9, tbl_10, tbl_11, tbl_12, tbl_13, tbl_14, tbl_15, tbl_16, tbl_17, tbl_18, tbl_19, tbl_20, tbl_21, tbl_22, tbl_23, tbl_24, tbl_25, W_top1, b_top1, W_top2, b_top2, W_top3):
    import jax
    import jax.numpy as jnp

    def _L0_rec_ref(dense_features, sparse_features):
        import jax, jax.numpy as jnp
        import numpy as np
        F = 26
        N = F + 1
        _TRIU_I, _TRIU_J = np.triu_indices(N, k=1)
        combined = jnp.concatenate([dense_features[:, None, :], sparse_features], axis=1)
        interactions = jnp.einsum('bnd,bmd->bnm', combined, combined)
        interactions_flat = interactions[:, _TRIU_I, _TRIU_J]
        return jnp.concatenate([dense_features, interactions_flat], axis=1)
    e = jnp.stack([tbl_0[ids[:, 0]], tbl_1[ids[:, 1]], tbl_2[ids[:, 2]], tbl_3[ids[:, 3]], tbl_4[ids[:, 4]], tbl_5[ids[:, 5]], tbl_6[ids[:, 6]], tbl_7[ids[:, 7]], tbl_8[ids[:, 8]], tbl_9[ids[:, 9]], tbl_10[ids[:, 10]], tbl_11[ids[:, 11]], tbl_12[ids[:, 12]], tbl_13[ids[:, 13]], tbl_14[ids[:, 14]], tbl_15[ids[:, 15]], tbl_16[ids[:, 16]], tbl_17[ids[:, 17]], tbl_18[ids[:, 18]], tbl_19[ids[:, 19]], tbl_20[ids[:, 20]], tbl_21[ids[:, 21]], tbl_22[ids[:, 22]], tbl_23[ids[:, 23]], tbl_24[ids[:, 24]], tbl_25[ids[:, 25]]], axis=1)
    z = _L0_rec_ref(r_dense_features, e)
    z = z.reshape(z.shape[0], -1)
    h = jnp.concatenate([z, r_dense_features], axis=1)
    h = jnp.maximum(h @ W_top1 + b_top1, 0.0)
    h = jnp.maximum(h @ W_top2 + b_top2, 0.0)
    y = h @ W_top3
    return y

_drawn_inputs = setup_inputs


def setup_inputs(seed=0):
    import zlib

    import numpy as np

    out = dict(_drawn_inputs(seed))
    spreads = {'b_top1': (0.0, 0.1), 'b_top2': (0.0, 0.1)}
    factors = {}
    for name, (base, spread) in spreads.items():
        noise = np.random.default_rng([zlib.crc32(name.encode()), seed]).standard_normal(out[name].shape)
        drawn = base * np.exp(spread * noise) if base else spread * noise
        out[name] = jnp.asarray(drawn.astype(out[name].dtype))
    for name, factor in factors.items():
        out[name] = (out[name] * factor).astype(out[name].dtype)
    return out
```

```python
from contextlib import ExitStack

import concourse.bass as bass
from concourse import mybir

F32 = mybir.dt.float32
I32 = mybir.dt.int32
ALU = mybir.AluOpType
ACT = mybir.ActivationFunctionType

P = 128
Q = 32
NQ = P // Q
HALF = Q // 2
FIELDS = 26
N = FIELDS + 1
COLS = N - 1
RUN = -(-COLS // NQ)
GROUPS = [(0, 4), (4, 4), (8, 4), (12, 4), (16, 4), (20, 4), (24, 2), (26, 1)]
OPEN = 1
PER_ENGINE = len(GROUPS) // 2


def quadrant_columns(g):
    return min(RUN, COLS - RUN * g)


def pair_row(c, k):
    return c * N - c * (c + 1) // 2 + k - c - 1


def dlrm(nc, dense, ids, tables, w1, b1, w2, b2, w3, out):
    batch = dense.shape[0]
    tiles = batch // P
    pairs = tiles // 2
    n1, n2 = w1.shape[1], w2.shape[1]
    t1, t2 = n1 // P, n2 // P
    npair = N * (N - 1) // 2

    dense_v = dense.rearrange("(p t) d -> p t d", t=tiles)
    ids_v = ids.rearrange("(p t) f -> p t f", t=tiles)

    ctx = ExitStack()
    with ctx:
        def sb(name, shape, dt=F32):
            return ctx.enter_context(nc.sbuf_tensor(name, shape, dt))

        def bank(name):
            return ctx.enter_context(nc.psum_tensor(name, [P, 512], F32))

        def sem(name):
            return ctx.enter_context(nc.semaphore(name))

        ids_ring = sb("ids_ring", [P, 2, FIELDS], I32)
        rows = sb("rows", [P, 2, N, P])
        vecs = sb("vecs", [P, P, N])
        dense_t = sb("dense_t", [P, P])
        pair_dots = sb("pair_dots", [P, RUN, P])
        w_pair = sb("w_pair", [P, RUN, n1])
        w_dense = sb("w_dense", [P, n1])
        w_again = sb("w_again", [P, n1])
        w2_sb = sb("w2_sb", [P, t1, n2])
        w3_sb = sb("w3_sb", [P, t2])
        b1_sb = sb("b1_sb", [P, t1])
        b2_sb = sb("b2_sb", [P, t2])
        h1 = sb("h1", [P, t1, P])
        h2 = sb("h2", [P, t2, P])
        y_sb = sb("y_sb", [P, tiles])
        ident = sb("ident", [P, P])

        turned = [bank(f"turned{i}") for i in range(2)]
        gram = [bank(f"gram{i}") for i in range(2)]
        acc = [bank(f"acc{i}") for i in range(2)]

        ids_loaded = [sem(f"ids_loaded{s}") for s in range(2)]
        dense_loaded = [sem(f"dense_loaded{s}") for s in range(2)]
        gathered = [[sem(f"gathered{s}_{f}") for f in range(FIELDS)] for s in range(2)]
        weights_cleared = sem("weights_cleared")
        weights_loaded = sem("weights_loaded")
        again_loaded = sem("again_loaded")
        weights_summed = sem("weights_summed")
        tiles_begun = sem("tiles_begun")
        ident_cleared = sem("ident_cleared")
        ident_ready = sem("ident_ready")
        grams_cleared = sem("grams_cleared")
        transposed = [sem(f"transposed{s}") for s in range(2)]
        placed = [sem("placed_by_vector"), sem("placed_by_scalar")]
        gram_done = sem("gram_done")
        spread = [sem("spread_by_scalar"), sem("spread_by_vector")]
        layer1_done = sem("layer1_done")
        relu1 = [sem("relu1_by_scalar"), sem("relu1_by_vector")]
        layer2_done = sem("layer2_done")
        relu2 = [sem("relu2_by_scalar"), sem("relu2_by_vector")]
        layer3_done = sem("layer3_done")
        y_kept = sem("y_kept")
        stored = sem("stored")

        block = ctx.enter_context(nc.Block())

        @block.sync
        def _(sp):
            with sp.Fori(0, pairs) as i:
                for s in range(2):
                    sp.wait_ge(transposed[s], i * len(GROUPS) + OPEN)
                    t = i * 2 + s
                    sp.dma_start(ids_ring[:, s, :], ids_v[:, bass.ds(t, 1), :]).then_inc(ids_loaded[s], 16)
                    sp.dma_start(rows[:, s, 0, :], dense_v[:, bass.ds(t, 1), :]).then_inc(dense_loaded[s], 16)
            sp.wait_ge(y_kept, tiles + OPEN)
            sp.dma_start(out.rearrange("(p t) o -> p (t o)", t=tiles), y_sb[:, :]).then_inc(stored, 16)
            sp.wait_ge(stored, 16)

        @block.gpsimd
        def _(pool):
            pool.memset(ident[:, :], 0.0).then_inc(ident_cleared, 1)
            pool.wait_ge(ident_cleared, 1)
            pool.affine_select(out=ident[:, :], in_=ident[:, :], compare_op=ALU.not_equal, fill=1.0, base=0,
                               pattern=[[-1, P]], channel_multiplier=1).then_inc(ident_ready, 1)
            with pool.Fori(0, pairs) as i:
                for s in range(2):
                    pool.wait_ge(ids_loaded[s], i * 16 + 16)
                    pool.sem_inc(tiles_begun, 1)
                    for f in range(FIELDS):
                        pool.indirect_dma_start(
                            out=rows[:, s, f + 1, :], out_offset=None, in_=tables[f],
                            in_offset=bass.IndirectOffsetOnAxis(ap=ids_ring[:, s, f:f + 1], axis=0),
                        ).then_inc(gathered[s][f], 16)

        def place(eng, copy, e, i, s):
            for m in range(PER_ENGINE):
                first, many = GROUPS[2 * m + e]
                eng.wait_ge(transposed[s], i * len(GROUPS) + OPEN + 2 * m + e + 1)
                src = turned[e][:, 0:many * P].rearrange("d (n p) -> d n p", n=many)
                if first == 0:
                    copy(dense_t[:, :], src[:, 0, :])
                copy(vecs[:, :, first:first + many].rearrange("d p n -> d n p"), src).then_inc(placed[e], 1)

        def spread_half(eng, copy, h, t):
            eng.wait_ge(gram_done, t * 2 + h + 1)
            for q in range(NQ):
                for g in range(NQ):
                    w = quadrant_columns(g)
                    src = gram[h][Q * q:Q * q + Q, 0:HALF * COLS].rearrange("k (p c) -> k c p", c=COLS)
                    last = copy(pair_dots[Q * g:Q * g + Q, 0:w, Q * q + HALF * h:Q * q + HALF * h + HALF],
                                src[:, RUN * g:RUN * g + w, :])
            last.then_inc(spread[h], 1)

        @block.vector
        def _(dve):
            for opened in (placed[0], spread[1], y_kept):
                dve.sem_inc(opened, OPEN)
            dve.memset(w_pair[:, :, :], 0.0).then_inc(weights_cleared, 1)
            for h in range(2):
                dve.memset(gram[h][:, :], 0.0).then_inc(grams_cleared, 1)
            dve.wait_ge(again_loaded, 32)
            dve.tensor_tensor(w_dense[:, :], w_dense[:, :], w_again[:, :], ALU.add).then_inc(weights_summed, 1)
            with dve.Fori(0, pairs) as i:
                for s in range(2):
                    t = i * 2 + s
                    place(dve, dve.tensor_copy, 0, i, s)
                    spread_half(dve, dve.tensor_copy, 1, t)
                    dve.wait_ge(layer1_done, t * 2 + 2)
                    for b in range(t1 // 2):
                        last = dve.tensor_scalar(h1[:, t1 // 2 + b, :], acc[1][:, b * P:(b + 1) * P],
                                                 b1_sb[:, t1 // 2 + b:t1 // 2 + b + 1], 0.0, ALU.add, ALU.max)
                    last.then_inc(relu1[1], 1)
                    dve.wait_ge(layer2_done, t * 2 + 2)
                    dve.tensor_scalar(h2[:, 1, :], acc[1][:, 0:P], b2_sb[:, 1:2], 0.0, ALU.add,
                                      ALU.max).then_inc(relu2[1], 1)
                    dve.wait_ge(layer3_done, t + 1)
                    dve.tensor_copy(y_sb[:, bass.ds(t, 1)], acc[0][:, P:P + 1]).then_inc(y_kept, 1)

        @block.scalar
        def _(act):
            for opened in (placed[1], spread[0]):
                act.sem_inc(opened, OPEN)
            act.dma_start(w_dense[:, :], w1[0:P, :]).then_inc(again_loaded, 16)
            act.dma_start(w_again[:, :], w1[P + npair:P + npair + P, :]).then_inc(again_loaded, 16)
            act.dma_start(b1_sb[:, :], b1.rearrange("(u p) -> p u", p=P), allow_slow_non_contiguous=True).then_inc(weights_loaded, 16)
            act.dma_start(b2_sb[:, :], b2.rearrange("(u p) -> p u", p=P), allow_slow_non_contiguous=True).then_inc(weights_loaded, 16)
            act.dma_start(w3_sb[:, :], w3.rearrange("(u p) o -> p (u o)", p=P), allow_slow_non_contiguous=True).then_inc(weights_loaded, 16)
            act.dma_start(w2_sb[:, :, :], w2.rearrange("(u p) n -> p u n", p=P)).then_inc(weights_loaded, 16)
            act.wait_ge(weights_cleared, 1)
            for c in range(COLS):
                g, j = c // RUN, c % RUN
                r = P + pair_row(c, c + 1)
                act.dma_start(w_pair[Q * g + c + 1:Q * g + N, j, :],
                              w1[r:r + N - 1 - c, :]).then_inc(weights_loaded, 16)
            act.wait_ge(weights_loaded, (4 + COLS) * 16)

            def copy(dst, src):
                return act.activation(dst, src, ACT.Copy)

            with act.Fori(0, pairs) as i:
                for s in range(2):
                    t = i * 2 + s
                    place(act, copy, 1, i, s)
                    spread_half(act, copy, 0, t)
                    act.wait_ge(layer1_done, t * 2 + 1)
                    for b in range(t1 // 2):
                        last = act.activation(h1[:, b, :], acc[0][:, b * P:(b + 1) * P], ACT.Relu,
                                              bias=b1_sb[:, b:b + 1])
                    last.then_inc(relu1[0], 1)
                    act.wait_ge(layer2_done, t * 2 + 1)
                    act.activation(h2[:, 0, :], acc[0][:, 0:P], ACT.Relu,
                                   bias=b2_sb[:, 0:1]).then_inc(relu2[0], 1)

        @block.tensor
        def _(pe):
            for opened in transposed:
                pe.sem_inc(opened, OPEN)
            pe.wait_ge(ident_ready, 1)
            pe.wait_ge(grams_cleared, 2)

            def transposes(i, s, t):
                for n, (first, many) in enumerate(GROUPS):
                    pe.wait_ge(placed[n % 2], t * PER_ENGINE + OPEN + n // 2)
                    for v in range(first, first + many):
                        if v == 0:
                            pe.wait_ge(dense_loaded[s], i * 16 + 16)
                        else:
                            pe.wait_ge(gathered[s][v - 1], i * 16 + 16)
                        last = pe.transpose(turned[n % 2][:, (v - first) * P:(v - first + 1) * P],
                                            rows[:, s, v, :], ident[:, :])
                    last.then_inc(transposed[s], 1)

            def grams(t):
                for e in range(2):
                    pe.wait_ge(placed[e], t * PER_ENGINE + OPEN + PER_ENGINE)
                for h in range(2):
                    pe.wait_ge(spread[h], t + OPEN)
                    for m in range(HALF):
                        for q in range(NQ):
                            p = Q * q + HALF * h + m
                            last = pe.matmul(gram[h][Q * q:Q * q + N, m * COLS:(m + 1) * COLS],
                                             vecs[:, p, :], vecs[:, p, 0:COLS], start=True, stop=True)
                    last.then_inc(gram_done, 1)

            def layers(t):
                for h in range(2):
                    pe.wait_ge(spread[h], t + OPEN + 1)
                pe.wait_ge(y_kept, t + OPEN)
                for u in range(t1):
                    a, col = acc[u // (t1 // 2)], u % (t1 // 2) * P
                    units = slice(u * P, (u + 1) * P)
                    pe.matmul(a[:, col:col + P], w_dense[:, units], dense_t[:, :], start=True, stop=False)
                    for j in range(RUN):
                        k = Q * sum(j < quadrant_columns(g) for g in range(NQ))
                        last = pe.matmul(a[:, col:col + P], w_pair[0:k, j, units], pair_dots[0:k, j, :],
                                         start=False, stop=(j == RUN - 1))
                    if u % (t1 // 2) == t1 // 2 - 1:
                        last.then_inc(layer1_done, 1)
                for e in range(2):
                    pe.wait_ge(relu1[e], t + 1)
                for v in range(t2):
                    for u in range(t1):
                        last = pe.matmul(acc[v][:, 0:P], w2_sb[:, u, v * P:(v + 1) * P], h1[:, u, :],
                                         start=(u == 0), stop=(u == t1 - 1))
                    last.then_inc(layer2_done, 1)
                for e in range(2):
                    pe.wait_ge(relu2[e], t + 1)
                for v in range(t2):
                    last = pe.matmul(acc[0][:, P:P + 1], h2[:, v, :], w3_sb[:, v:v + 1],
                                     start=(v == 0), stop=(v == t2 - 1))
                last.then_inc(layer3_done, 1)

            with pe.Fori(0, pairs) as i:
                for s in range(2):
                    t = i * 2 + s
                    transposes(i, s, t)
                    grams(t)
                    if s == 0:
                        pe.wait_ge(weights_summed, 1)
                        pe.wait_ge(weights_loaded, (4 + COLS) * 16)
                    layers(t)


def kernel(**inputs):
    import numpy as _np
    import concourse.bacc as _bacc
    from concourse.bass_utils import run_bass_kernel_spmd as _run

    nc = _bacc.Bacc("TRN2", target_bir_lowering=False, num_devices=1)
    arrays, args = {}, {}
    for name in inputs:
        a = _np.ascontiguousarray(inputs[name])
        arrays[f"in_{name}_dram"] = a
        args[name] = nc.dram_tensor(f"in_{name}_dram", a.shape, mybir.dt.from_np(a.dtype),
                                    kind="ExternalInput").ap()
    batch = inputs["r_dense_features"].shape[0]
    out = nc.dram_tensor("out_dram", (batch, 1), F32, kind="ExternalOutput").ap()
    dlrm(nc, args["r_dense_features"], args["ids"], [args[f"tbl_{f}"] for f in range(FIELDS)],
         args["W_top1"], args["b_top1"], args["W_top2"], args["b_top2"], args["W_top3"], out)
    r = _run(nc, [arrays], core_ids=[0])
    return r.results[0]["out_dram"]
```

```python
from contextlib import ExitStack

import concourse.bass as bass
from concourse import mybir

F32 = mybir.dt.float32
F32R = mybir.dt.float32r
F16 = mybir.dt.float16
I32 = mybir.dt.int32
ALU = mybir.AluOpType
ACT = mybir.ActivationFunctionType

P = 128
Q = 32
NQ = P // Q
HALF = Q // 2
FIELDS = 26
N = FIELDS + 1
COLS = N - 1
RUN = -(-COLS // NQ)
FOUND = [1, 5, 11, 16, 17, 22, 24, 25]
CHUNKS = 8
GROUPS = [(0, 2), (3, 3), (7, 4), (11, 1), (13, 4), (19, 2), (21, 2), (24, 1)]
NG = len(GROUPS)
GATHERED = [v - 1 for first, many in GROUPS for v in range(first, first + many) if v]
assert sorted(FOUND + GATHERED) == list(range(FIELDS))

AFTER_PICK = {3: [0, 1], 4: [2, 3], 5: [4, 5], 6: [6, 7], 7: []}
AFTER_PICKS = [0, 1, 2]
AFTER_GRAMS = [[3], [0, 1], [0, 1]]
AFTER_BLOCK = [[[4], [5], [6], []], [[2, 3], [4], [5], [6]], [[2], [3], [4], [5]]]
AFTER_LAYER2 = [[7], [7], [6]]
AFTER_LAYER3 = [[], [], [7]]


def quadrant_columns(g):
    return min(RUN, COLS - RUN * g)


def pair_row(c, k):
    return c * N - c * (c + 1) // 2 + k - c - 1


def dlrm(nc, dense, ids, tables, w1, b1, w2, b2, w3, out):
    batch = dense.shape[0]
    tiles = batch // P
    n1, n2 = w1.shape[1], w2.shape[1]
    u1, u2 = n1 // P, n2 // P
    half = u1 // 2
    npair = N * (N - 1) // 2
    height = tables[FOUND[0]].shape[0] // CHUNKS

    ctx = ExitStack()
    with ctx:
        def sb(name, shape, dt=F32):
            return ctx.enter_context(nc.sbuf_tensor(name, shape, dt))

        def bank(name):
            return ctx.enter_context(nc.psum_tensor(name, [P, 512], F32))

        def sem(name):
            return ctx.enter_context(nc.semaphore(name))

        ids_sb = sb("ids_sb", [P, tiles, FIELDS], I32)
        ids16 = sb("ids16", [P, tiles, len(FOUND)], F16)
        dense_sb = sb("dense_sb", [P, tiles, P])
        rows = sb("rows", [P, tiles, len(GATHERED), P])
        vecs = sb("vecs", [P, tiles, P, N])
        dense_t = sb("dense_t", [P, tiles, P])
        pair_dots = sb("pair_dots", [P, RUN, P])
        h1 = sb("h1", [P, u1, P])
        h2 = sb("h2", [P, u2, P])
        y_sb = sb("y_sb", [P, tiles])
        row_int = sb("row_int", [P, CHUNKS], I32)
        row = sb("row", [P, CHUNKS])
        table = sb("table", [height, 2, CHUNKS * P])
        high = sb("high", [height, 2, CHUNKS * P], F32R)
        low = sb("low", [height, 2, CHUNKS * P], F32R)
        wanted = sb("wanted", [P, 2, batch], F16)
        onehot = sb("onehot", [height, 2, CHUNKS, batch], F32R)
        minus_row = sb("minus_row", [P, CHUNKS])
        distance = sb("distance", [height, batch])
        one = sb("one", [P, 1])
        w_pair = sb("w_pair", [P, RUN, n1])
        w_dense = sb("w_dense", [P, n1])
        w_again = sb("w_again", [P, n1])
        w2_sb = sb("w2_sb", [P, u1, n2])
        w3_sb = sb("w3_sb", [P, u2])
        b1_sb = sb("b1_sb", [P, u1])
        b2_sb = sb("b2_sb", [P, u2])
        zero = sb("zero", [P, 1])
        ident = sb("ident", [P, P])
        ident16 = sb("ident16", [P, P], F16)

        turned = [bank(f"turned{i}") for i in range(2)]
        gram = [bank(f"gram{i}") for i in range(2)]
        acc = [bank(f"acc{i}") for i in range(2)]
        top = [bank(f"top{i}") for i in range(2)]
        sent_ids, picked = acc, top

        ids_loaded = sem("ids_loaded")
        dense_loaded = sem("dense_loaded")
        table_loaded = [sem(f"table_loaded{s}") for s in range(2)]
        w1_dense_loaded = sem("w1_dense_loaded")
        weights_loaded = sem("weights_loaded")
        gathered = {f: sem(f"gathered{f}") for f in GATHERED}
        zero_made = sem("zero_made")
        weights_cleared = sem("weights_cleared")
        weights_summed = sem("weights_summed")
        ident_cleared = sem("ident_cleared")
        ident_made = sem("ident_made")
        ident16_made = sem("ident16_made")
        row_int_made = sem("row_int_made")
        row_made = sem("row_made")
        ids16_made = sem("ids16_made")
        grams_cleared = sem("grams_cleared")
        ids_sent = sem("ids_sent")
        wanted_made = sem("wanted_made")
        high_made = sem("high_made")
        low_made = sem("low_made")
        onehot_made = sem("onehot_made")
        minus_row_made = sem("minus_row_made")
        distance_made = sem("distance_made")
        last_chunk_made = sem("last_chunk_made")
        rows_picked = sem("rows_picked")
        picked_placed = sem("picked_placed")
        transposed = sem("transposed")
        placed = [sem(f"placed_from_bank{b}") for b in range(2)]
        gram_done = sem("gram_done")
        spread = [sem("spread_by_vector"), sem("spread_by_scalar")]
        layer1_done = sem("layer1_done")
        relu1 = [sem("relu1_by_scalar"), sem("relu1_by_vector")]
        layer2_done = sem("layer2_done")
        relu2 = [sem("relu2_by_scalar"), sem("relu2_by_vector")]
        layer3_done = sem("layer3_done")
        y_kept = sem("y_kept")
        stored = sem("stored")

        MISC = 4

        block = ctx.enter_context(nc.Block())

        @block.sync
        def _(sp):
            def load_table(m):
                if m >= 2:
                    sp.wait_ge(low_made, m - 1)
                sp.dma_start(table[:, m % 2, :], tables[FOUND[m]].rearrange("(p c) d -> p (c d)", c=CHUNKS)
                             ).then_inc(table_loaded[m % 2], 16)

            def load_pairs(columns):
                for c in columns:
                    g, j = c // RUN, c % RUN
                    r = P + pair_row(c, c + 1)
                    sp.dma_start(w_pair[Q * g + c + 1:Q * g + N, j, :],
                                 w1[r:r + N - 1 - c, :]).then_inc(weights_loaded, 16)

            sp.dma_start(ids_sb[:, :, :], ids.rearrange("(p t) f -> p t f", t=tiles)).then_inc(ids_loaded, 16)
            load_table(0)
            load_table(1)
            sp.dma_start(dense_sb[:, :, :], dense.rearrange("(p t) d -> p t d", t=tiles)).then_inc(dense_loaded, 16)
            sp.wait_ge(weights_cleared, 1)
            share = -(-COLS // (len(FOUND) - 2))
            for m in range(2, len(FOUND)):
                load_table(m)
                load_pairs(range(share * (m - 2), min(share * (m - 1), COLS)))
            sp.dma_start(w_dense[:, :], w1[0:P, :]).then_inc(w1_dense_loaded, 16)
            sp.dma_start(w_again[:, :], w1[P + npair:P + npair + P, :]).then_inc(w1_dense_loaded, 16)
            sp.dma_start(b1_sb[:, :], b1.rearrange("(u p) -> p u", p=P), allow_slow_non_contiguous=True
                         ).then_inc(weights_loaded, 16)
            sp.dma_start(b2_sb[:, :], b2.rearrange("(u p) -> p u", p=P), allow_slow_non_contiguous=True
                         ).then_inc(weights_loaded, 16)
            sp.dma_start(w3_sb[:, :], w3.rearrange("(u p) o -> p (u o)", p=P), allow_slow_non_contiguous=True
                         ).then_inc(weights_loaded, 16)
            sp.dma_start(w2_sb[:, :, :], w2.rearrange("(u p) n -> p u n", p=P)).then_inc(weights_loaded, 16)
            sp.wait_ge(y_kept, tiles)
            sp.dma_start(out.rearrange("(p t) o -> p (t o)", t=tiles), y_sb[:, :]).then_inc(stored, 16)
            sp.wait_ge(stored, 16)

        @block.gpsimd
        def _(pool):
            pool.memset(ident[:, :], 0.0).then_inc(ident_cleared, 1)
            pool.wait_ge(ident_cleared, 1)
            pool.affine_select(out=ident[:, :], in_=ident[:, :], compare_op=ALU.not_equal, fill=1.0, base=0,
                               pattern=[[-1, P]], channel_multiplier=1).then_inc(ident_made, 1)
            pool.iota(row_int[:, :], pattern=[[1, CHUNKS]], base=0,
                      channel_multiplier=CHUNKS).then_inc(row_int_made, 1)
            pool.wait_ge(ids_loaded, 16)
            for t in range(tiles):
                for n, f in enumerate(GATHERED):
                    if t:
                        pool.wait_ge(gathered[f], 16 * t)
                    pool.indirect_dma_start(
                        out=rows[:, t, n, :], out_offset=None, in_=tables[f],
                        in_offset=bass.IndirectOffsetOnAxis(ap=ids_sb[:, t, f:f + 1], axis=0),
                    ).then_inc(gathered[f], 16)

        def place(eng, copy, t, n):
            first, many = GROUPS[n]
            eng.wait_ge(transposed, t * NG + n + 1)
            src = turned[n % 2][:, 0:many * P].rearrange("d (n p) -> d n p", n=many)
            if first == 0:
                copy(dense_t[:, t, :], src[:, 0, :])
            copy(vecs[:, t, :, first:first + many].rearrange("d p n -> d n p"), src).then_inc(placed[n % 2], 1)

        def spread_columns(eng, copy, e, t):
            for h in range(2):
                eng.wait_ge(gram_done, t * 2 + h + 1)
                for q in (2 * e, 2 * e + 1):
                    src = gram[h][Q * q:Q * q + Q, 0:HALF * COLS].rearrange("k (p c) -> k c p", c=COLS)
                    for g in range(NQ):
                        w = quadrant_columns(g)
                        last = copy(pair_dots[Q * g:Q * g + Q, 0:w, Q * q + HALF * h:Q * q + HALF * h + HALF],
                                    src[:, RUN * g:RUN * g + w, :])
                last.then_inc(spread[e], 1)

        @block.vector
        def _(dve):
            dve.memset(zero[:, :], 0.0).then_inc(zero_made, 1)
            dve.memset(one[:, :], 1.0).then_inc(minus_row_made, 1)
            for h in range(2):
                dve.memset(gram[h][:, :], 0.0).then_inc(grams_cleared, 1)
            dve.wait_ge(ident_made, 1)
            dve.tensor_copy(ident16[:, :], ident[:, :]).then_inc(ident16_made, 1)
            dve.wait_ge(row_int_made, 1)
            dve.tensor_copy(row[:, :], row_int[:, :]).then_inc(row_made, 1)
            dve.tensor_scalar(minus_row[:, :], row_int[:, :], -1.0, None, ALU.mult).then_inc(minus_row_made, 1)
            dve.wait_ge(ids_loaded, 16)
            for m, f in enumerate(FOUND):
                last = dve.tensor_copy(ids16[:, :, m], ids_sb[:, :, f])
            last.then_inc(ids16_made, 1)
            dve.wait_ge(row_made, 1)
            for m in range(len(FOUND)):
                dve.wait_ge(high_made, m + 1)
                if m >= 2:
                    dve.wait_ge(rows_picked, m - 1)
                dve.tensor_tensor(low[:, m % 2, :], table[:, m % 2, :], high[:, m % 2, :],
                                  ALU.subtract).then_inc(low_made, 1)
                dve.wait_ge(wanted_made, m + 1)
                for c in range(CHUNKS - 1):
                    dve.tensor_scalar(onehot[:, m % 2, c, :], wanted[0:height, m % 2, :], row[0:height, c:c + 1],
                                      None, ALU.is_equal).then_inc(onehot_made, 1)
            dve.wait_ge(w1_dense_loaded, 32)
            dve.tensor_tensor(w_dense[:, :], w_dense[:, :], w_again[:, :], ALU.add).then_inc(weights_summed, 1)
            dve.wait_ge(weights_loaded, (MISC + COLS) * 16)

            def place_mine(t, groups):
                for n in groups:
                    if n % 2 == 0:
                        place(dve, dve.tensor_copy, t, n)

            place_mine(1, AFTER_PICKS)
            for t in range(tiles):
                spread_columns(dve, dve.tensor_copy, 0, t)
                if t + 1 < tiles:
                    place_mine(t + 1, AFTER_GRAMS[t] + sum(AFTER_BLOCK[t], []))
                dve.wait_ge(layer1_done, t * 2 + 2)
                for u in range(half, u1):
                    last = dve.tensor_scalar(h1[:, u, :], acc[1][:, (u - half) * P:(u - half + 1) * P],
                                             b1_sb[:, u:u + 1], 0.0, ALU.add, ALU.max)
                last.then_inc(relu1[1], 1)
                dve.wait_ge(layer2_done, t * 2 + 2)
                dve.tensor_scalar(h2[:, 1, :], top[1][:, 0:P], b2_sb[:, 1:2], 0.0, ALU.add,
                                  ALU.max).then_inc(relu2[1], 1)
                if t + 1 < tiles:
                    place_mine(t + 1, AFTER_LAYER2[t])
                dve.wait_ge(layer3_done, t + 1)
                dve.tensor_copy(y_sb[:, t:t + 1], top[0][:, P:P + 1]).then_inc(y_kept, 1)
                if t + 1 < tiles:
                    place_mine(t + 1, AFTER_LAYER3[t])

        @block.scalar
        def _(act):
            def copy(dst, src):
                return act.activation(dst, src, ACT.Copy)

            def place_picked(m):
                act.wait_ge(rows_picked, m + 1)
                v = FOUND[m] + 1
                copy(vecs[:, :, :, v].rearrange("d t p -> d (t p)"),
                     picked[m % 2][:, :]).then_inc(picked_placed, 1)
                for n in AFTER_PICK.get(m, []):
                    place(act, copy, 0, n)

            for m in range(len(FOUND)):
                act.wait_ge(ids_sent, m + 1)
                if m >= 2:
                    act.wait_ge(onehot_made, (m - 1) * (CHUNKS - 1))
                copy(wanted[:, m % 2, :], sent_ids[m % 2][:, :]).then_inc(wanted_made, 1)
                act.wait_ge(table_loaded[m % 2], m // 2 * 16 + 16)
                if m >= 2:
                    act.wait_ge(rows_picked, m - 1)
                copy(high[:, m % 2, :], table[:, m % 2, :]).then_inc(high_made, 1)
                act.wait_ge(minus_row_made, 2)
                act.wait_ge(wanted_made, m + 1)
                act.activation(distance[:, :], wanted[0:height, m % 2, :], ACT.Abs,
                               bias=minus_row[0:height, CHUNKS - 1:CHUNKS]).then_inc(distance_made, 1)
                act.wait_ge(distance_made, m + 1)
                act.activation(onehot[:, m % 2, CHUNKS - 1, :], distance[:, :], ACT.Relu, scale=-1.0,
                               bias=one[0:height, :]).then_inc(last_chunk_made, 1)
                if m >= 1:
                    place_picked(m - 1)
                else:
                    act.wait_ge(zero_made, 1)
                    copy(w_pair[:, :, :].rearrange("p j n -> p (j n)"),
                         zero[:, 0:1].to_broadcast([P, RUN * n1])).then_inc(weights_cleared, 1)
            place_picked(len(FOUND) - 1)
            act.wait_ge(weights_loaded, (MISC + COLS) * 16)

            def place_mine(t, groups):
                for n in groups:
                    if n % 2 == 1:
                        place(act, copy, t, n)

            place_mine(1, AFTER_PICKS)
            for t in range(tiles):
                spread_columns(act, copy, 1, t)
                if t + 1 < tiles:
                    place_mine(t + 1, AFTER_GRAMS[t] + sum(AFTER_BLOCK[t][:half], []))
                act.wait_ge(layer1_done, t * 2 + 1)
                for u in range(half):
                    last = act.activation(h1[:, u, :], acc[0][:, u * P:(u + 1) * P], ACT.Relu,
                                          bias=b1_sb[:, u:u + 1])
                last.then_inc(relu1[0], 1)
                if t + 1 < tiles:
                    place_mine(t + 1, sum(AFTER_BLOCK[t][half:], []))
                act.wait_ge(layer2_done, t * 2 + 1)
                act.activation(h2[:, 0, :], top[0][:, 0:P], ACT.Relu, bias=b2_sb[:, 0:1]).then_inc(relu2[0], 1)
                if t + 1 < tiles:
                    place_mine(t + 1, AFTER_LAYER2[t] + AFTER_LAYER3[t])

        @block.tensor
        def _(pe):
            def send_ids(m):
                if m >= 2:
                    pe.wait_ge(wanted_made, m - 1)
                for t in range(tiles):
                    last = pe.matmul(sent_ids[m % 2][:, t * P:(t + 1) * P],
                                     ids16[:, t, m:m + 1].to_broadcast([P, P]), ident16[:, :], start=True, stop=True)
                last.then_inc(ids_sent, 1)

            def pick(m):
                pe.wait_ge(low_made, m + 1)
                if m >= 2:
                    pe.wait_ge(picked_placed, m - 1)
                for c in range(CHUNKS):
                    if c < CHUNKS - 1:
                        pe.wait_ge(onehot_made, m * (CHUNKS - 1) + c + 1)
                    else:
                        pe.wait_ge(last_chunk_made, m + 1)
                    for part in (high, low):
                        last = pe.matmul(picked[m % 2][:, :], part[:, m % 2, c * P:(c + 1) * P],
                                         onehot[:, m % 2, c, :], start=(c == 0 and part is high),
                                         stop=(c == CHUNKS - 1 and part is low))
                last.then_inc(rows_picked, 1)

            def transposes(t, groups):
                for n in groups:
                    first, many = GROUPS[n]
                    if t or n >= 2:
                        pe.wait_ge(placed[n % 2], (t * NG + n) // 2)
                    for v in range(first, first + many):
                        if v == 0:
                            pe.wait_ge(dense_loaded, 16)
                            src = dense_sb[:, t, :]
                        else:
                            pe.wait_ge(gathered[v - 1], 16 * (t + 1))
                            src = rows[:, t, GATHERED.index(v - 1), :]
                        last = pe.transpose(turned[n % 2][:, (v - first) * P:(v - first + 1) * P], src, ident[:, :])
                    last.then_inc(transposed, 1)

            def grams(t):
                pe.wait_ge(picked_placed, len(FOUND))
                for b in range(2):
                    pe.wait_ge(placed[b], (t + 1) * NG // 2)
                if t:
                    for e in range(2):
                        pe.wait_ge(spread[e], t * 2)
                for h in range(2):
                    for m in range(HALF):
                        for q in range(NQ):
                            p = Q * q + HALF * h + m
                            last = pe.matmul(gram[h][Q * q:Q * q + N, m * COLS:(m + 1) * COLS],
                                             vecs[:, t, p, :], vecs[:, t, p, 0:COLS], start=True, stop=True)
                    last.then_inc(gram_done, 1)

            def layers(t):
                following = t + 1 < tiles
                if t:
                    pe.wait_ge(y_kept, t)
                for u in range(u1):
                    pe.matmul(acc[u // half][:, u % half * P:(u % half + 1) * P], w_dense[:, u * P:(u + 1) * P],
                              dense_t[:, t, :], start=(u % half == 0), stop=False, skip_group_check=True)
                if following:
                    transposes(t + 1, AFTER_GRAMS[t])
                for e in range(2):
                    pe.wait_ge(spread[e], t * 2 + 2)
                for u in range(u1):
                    for j in range(RUN):
                        k = Q * sum(j < quadrant_columns(g) for g in range(NQ))
                        last = pe.matmul(acc[u // half][:, u % half * P:(u % half + 1) * P],
                                         w_pair[0:k, j, u * P:(u + 1) * P], pair_dots[0:k, j, :],
                                         start=False, stop=(j == RUN - 1), skip_group_check=True)
                    if u % half == half - 1:
                        last.then_inc(layer1_done, 1)
                    if following:
                        transposes(t + 1, AFTER_BLOCK[t][u])

                def layer2(v, blocks):
                    for u in blocks:
                        last = pe.matmul(top[v][:, 0:P], w2_sb[:, u, v * P:(v + 1) * P], h1[:, u, :],
                                         start=(u == 0), stop=(u == u1 - 1))
                    return last

                pe.wait_ge(relu1[0], t + 1)
                for v in range(u2):
                    layer2(v, range(half))
                pe.wait_ge(relu1[1], t + 1)
                for v in range(u2):
                    layer2(v, range(half, u1)).then_inc(layer2_done, 1)
                if following:
                    transposes(t + 1, AFTER_LAYER2[t])
                for v in range(u2):
                    pe.wait_ge(relu2[v], t + 1)
                    last = pe.matmul(top[0][:, P:P + 1], h2[:, v, :], w3_sb[:, v:v + 1],
                                     start=(v == 0), stop=(v == u2 - 1))
                last.then_inc(layer3_done, 1)
                if following:
                    transposes(t + 1, AFTER_LAYER3[t])

            pe.wait_ge(ident16_made, 1)
            pe.wait_ge(ids16_made, 1)
            send_ids(0)
            for m in range(len(FOUND)):
                if m + 1 < len(FOUND):
                    send_ids(m + 1)
                pick(m)
                transposes(0, AFTER_PICK.get(m, []))
            transposes(1, AFTER_PICKS)
            pe.wait_ge(grams_cleared, 2)
            for t in range(tiles):
                grams(t)
                if t == 0:
                    pe.wait_ge(weights_summed, 1)
                    pe.wait_ge(weights_loaded, (MISC + COLS) * 16)
                layers(t)


def kernel(**inputs):
    import numpy as _np
    import concourse.bacc as _bacc
    from concourse.bass_utils import run_bass_kernel_spmd as _run

    nc = _bacc.Bacc("TRN2", target_bir_lowering=False, num_devices=1)
    arrays, args = {}, {}
    for name in inputs:
        a = _np.ascontiguousarray(inputs[name])
        arrays[f"in_{name}_dram"] = a
        args[name] = nc.dram_tensor(f"in_{name}_dram", a.shape, mybir.dt.from_np(a.dtype),
                                    kind="ExternalInput").ap()
    batch = inputs["r_dense_features"].shape[0]
    out = nc.dram_tensor("out_dram", (batch, 1), F32, kind="ExternalOutput").ap()
    dlrm(nc, args["r_dense_features"], args["ids"], [args[f"tbl_{f}"] for f in range(FIELDS)],
         args["W_top1"], args["b_top1"], args["W_top2"], args["b_top2"], args["W_top3"], out)
    r = _run(nc, [arrays], core_ids=[0])
    return r.results[0]["out_dram"]
```

```python
from contextlib import ExitStack

import concourse.bass as bass
from concourse import mybir

F32 = mybir.dt.float32
F32R = mybir.dt.float32r
F16 = mybir.dt.float16
I32 = mybir.dt.int32
ALU = mybir.AluOpType
ACT = mybir.ActivationFunctionType

P = 128
Q = 32
NQ = P // Q
HALF = Q // 2
FIELDS = 26
N = FIELDS + 1
FOLD = N // 2
SLOTS = N - FOLD
RUN = -(-SLOTS // NQ)
FOUND = [1, 5, 11, 16, 17, 22, 24, 25]
LATE = 23
CHUNKS = [8] * len(FOUND) + [10]
GROUPS = [(7, 4), (3, 3), (0, 2), (21, 2), (13, 4), (19, 2), (11, 1), (24, 1)]
GATHERED = [v - 1 for first, many in GROUPS for v in range(first, first + many) if v]
assert sorted(FOUND + GATHERED) == list(range(FIELDS))

WARM_UP = (13, 18)

AFTER_PICK = {1: [0, 1], 2: [2, 3], 3: [4, 5], 4: [6, 7]}
AFTER_PICKS = [0, 1]
AFTER_DENSE = [[2, 3], [0, 1], [0, 1]]
AFTER_BLOCK = [[[4, 5], [6], [], []], [[2, 3], [4, 5], [6], []], [[2, 3], [4], [5], [6]]]


def groups_before(t, n, b=None):
    each = [len(GROUPS)] + [len(GROUPS) - 1] * (t - 1) if t else []
    return sum(len([i for i in range(many) if b is None or i % 2 == b]) for many in each + [n])


def quadrant_slots(g):
    return min(RUN, SLOTS - RUN * g)


def laid_over(r, s):
    return s >= 1 and s <= r < s + FOLD


def pair_row(r, s):
    if s == 0 and r <= FOLD:
        return None
    c = s - 1 if laid_over(r, s) else FOLD + s
    lo, hi = min(r, c), max(r, c)
    return None if lo == hi else lo * N - lo * (lo + 1) // 2 + hi - lo - 1


def dlrm(nc, dense, ids, tables, w1, pair_weights, over_rows, b1, w2, b2, w3, out):
    batch = dense.shape[0]
    tiles = batch // P
    n1, n2 = w1.shape[1], w2.shape[1]
    u1, u2 = n1 // P, n2 // P
    half = u1 // 2
    npair = N * (N - 1) // 2
    found = FOUND + [LATE]
    height = tables[LATE].shape[0] // CHUNKS[-1]
    assert all(tables[f].shape[0] == height * chunks for f, chunks in zip(found, CHUNKS))
    first_tile = [0] * len(FOUND) + [1]
    width = [batch - P * t for t in first_tile]
    made_rows = max(n * w for n, w in zip(CHUNKS, width))

    ctx = ExitStack()
    with ctx:
        def sb(name, shape, dt=F32):
            return ctx.enter_context(nc.sbuf_tensor(name, shape, dt))

        def bank(name):
            return ctx.enter_context(nc.psum_tensor(name, [P, 512], F32))

        def sem(name):
            return ctx.enter_context(nc.semaphore(name))

        ids_sb = sb("ids_sb", [P, tiles, FIELDS], I32)
        ids16 = sb("ids16", [P, tiles, len(found)], F16)
        dense_sb = sb("dense_sb", [P, tiles, P])
        rows = sb("rows", [P, tiles, len(GATHERED), P])
        vecs = sb("vecs", [P, tiles, P, N])
        dense_t = sb("dense_t", [P, tiles, P])
        pair_dots = sb("pair_dots", [P, RUN, P])
        h1 = sb("h1", [P, u1, P])
        h2 = sb("h2", [P, u2, P])
        y_sb = sb("y_sb", [1, P, tiles])
        row_int = sb("row_int", [P, 2, max(CHUNKS)], I32)
        row = sb("row", [P, 2, max(CHUNKS)])
        minus_row = sb("minus_row", [P, 2, max(CHUNKS)])
        table = sb("table", [height, 2, max(CHUNKS) * P])
        high = sb("high", [height, 2, max(CHUNKS) * P], F32R)
        low = sb("low", [height, 2, max(CHUNKS) * P], F32R)
        wanted = sb("wanted", [P, 2, batch], F16)
        onehot = sb("onehot", [height, 2, made_rows], F32R)
        one = sb("one", [height, 1])
        distance = sb("distance", [height, batch])
        w_pair = sb("w_pair", [P, RUN, n1])
        over = sb("over", [P, RUN], I32)
        w_dense = sb("w_dense", [P, n1])
        w_again = sb("w_again", [P, n1])
        w2_sb = sb("w2_sb", [P, u1, n2])
        w3_sb = sb("w3_sb", [P, u2])
        b1_sb = sb("b1_sb", [P, u1])
        b2_sb = sb("b2_sb", [P, u2])
        ident = sb("ident", [P, P])
        ident16 = sb("ident16", [P, P], F16)

        turned = [bank(f"turned{i}") for i in range(2)]
        gram = [bank(f"gram{i}") for i in range(2)]
        acc = [bank(f"acc{i}") for i in range(2)]
        top = [bank(f"top{i}") for i in range(2)]
        sent_ids, picked = acc, top

        ids_loaded = sem("ids_loaded")
        dense_loaded = sem("dense_loaded")
        first_half_loaded = sem("first_half_loaded")
        table_loaded = [sem(f"table_loaded{s}") for s in range(2)]
        w1_dense_loaded = sem("w1_dense_loaded")
        weights_loaded = sem("weights_loaded")
        over_loaded = sem("over_loaded")
        gathered = {f: sem(f"gathered{f}") for f in GATHERED}
        weights_summed = sem("weights_summed")
        ident_cleared = sem("ident_cleared")
        ident_made = sem("ident_made")
        ident16_made = sem("ident16_made")
        row_int_made = sem("row_int_made")
        row_made = sem("row_made")
        ids16_made = sem("ids16_made")
        grams_cleared = sem("grams_cleared")
        ids_sent = sem("ids_sent")
        wanted_made = sem("wanted_made")
        high_made = sem("high_made")
        low_made = sem("low_made")
        onehot_made = sem("onehot_made")
        minus_row_made = sem("minus_row_made")
        one_made = sem("one_made")
        distance_made = sem("distance_made")
        last_chunk_made = sem("last_chunk_made")
        rows_picked = sem("rows_picked")
        picked_placed = sem("picked_placed")
        transposed = sem("transposed")
        placed = [sem(f"placed_from_bank{b}") for b in range(2)]
        gram_done = sem("gram_done")
        laid_under = sem("laid_under")
        laid_over_all = sem("laid_over_all")
        layer1_done = sem("layer1_done")
        relu1 = [sem("relu1_by_scalar"), sem("relu1_by_vector")]
        layer2_done = sem("layer2_done")
        relu2 = sem("relu2")
        layer3_done = sem("layer3_done")
        y_kept = sem("y_kept")
        stored = sem("stored")

        WEIGHTS = 4 + RUN

        block = ctx.enter_context(nc.Block())

        def parts(m):
            columns = CHUNKS[m] * P
            return [slice(0, columns // 2), slice(columns // 2, columns)] if m == 0 else [slice(0, columns)]

        def parts_through(m):
            return sum(len(parts(i)) for i in range(m + 1))

        def vector_chunks_before(m):
            return sum(n - 1 for n in CHUNKS[:m])

        def chunk_rows(m, c):
            return onehot[:, m % 2, c * width[m]:(c + 1) * width[m]]

        @block.sync
        def _(sp):
            def load_table(m):
                if m >= 2:
                    sp.wait_ge(low_made, parts_through(m - 2))
                rows_of = tables[found[m]].rearrange("(p c) d -> p (c d)", c=CHUNKS[m])
                for n, columns in enumerate(parts(m)):
                    loaded = first_half_loaded if n < len(parts(m)) - 1 else table_loaded[m % 2]
                    sp.dma_start(table[:, m % 2, columns], rows_of[:, columns]).then_inc(loaded, 16)

            sp.dma_start(ids_sb[:, :, :], ids.rearrange("(p t) f -> p t f", t=tiles)).then_inc(ids_loaded, 16)
            load_table(0)
            load_table(1)
            sp.dma_start(dense_sb[:, :, :], dense.rearrange("(p t) d -> p t d", t=tiles)).then_inc(dense_loaded, 16)
            sp.dma_start(over[:, :], over_rows).then_inc(over_loaded, 16)
            for m in range(2, len(found)):
                load_table(m)
                if m < 2 + RUN:
                    sp.dma_start(w_pair[:, m - 2, :], pair_weights[:, m - 2, :]).then_inc(weights_loaded, 16)
            sp.dma_start(w_dense[:, :], w1[0:P, :]).then_inc(w1_dense_loaded, 16)
            sp.dma_start(w_again[:, :], w1[P + npair:P + npair + P, :]).then_inc(w1_dense_loaded, 16)
            sp.dma_start(b1_sb[:, :], b1.rearrange("(u p) -> p u", p=P), allow_slow_non_contiguous=True
                         ).then_inc(weights_loaded, 16)
            sp.dma_start(b2_sb[:, :], b2.rearrange("(u p) -> p u", p=P), allow_slow_non_contiguous=True
                         ).then_inc(weights_loaded, 16)
            sp.dma_start(w3_sb[:, :], w3.rearrange("(u p) o -> p (u o)", p=P), allow_slow_non_contiguous=True
                         ).then_inc(weights_loaded, 16)
            sp.dma_start(w2_sb[:, :, :], w2.rearrange("(u p) n -> p u n", p=P)).then_inc(weights_loaded, 16)
            sp.wait_ge(y_kept, tiles)
            sp.dma_start(out.rearrange("s o -> o s"), y_sb[:, :, :].rearrange("o p t -> o (p t)")).then_inc(stored, 16)
            sp.wait_ge(stored, 16)

        @block.gpsimd
        def _(pool):
            pool.memset(ident[:, :], 0.0).then_inc(ident_cleared, 1)
            pool.wait_ge(ident_cleared, 1)
            pool.affine_select(out=ident[:, :], in_=ident[:, :], compare_op=ALU.not_equal, fill=1.0, base=0,
                               pattern=[[-1, P]], channel_multiplier=1).then_inc(ident_made, 1)
            for kind, chunks in enumerate((CHUNKS[0], CHUNKS[-1])):
                pool.iota(row_int[:, kind, :], pattern=[[1, max(CHUNKS)]], base=0,
                          channel_multiplier=chunks).then_inc(row_int_made, 1)
            pool.wait_ge(ids_loaded, 16)
            for t in range(tiles):
                for n, f in enumerate(GATHERED):
                    if t and f == LATE:
                        continue
                    if t:
                        pool.wait_ge(gathered[f], 16 * t)
                    pool.indirect_dma_start(
                        out=rows[:, t, n, :], out_offset=None, in_=tables[f],
                        in_offset=bass.IndirectOffsetOnAxis(ap=ids_sb[:, t, f:f + 1], axis=0),
                    ).then_inc(gathered[f], 16)

        def place(eng, copy, t, n):
            first, many = GROUPS[n]
            eng.wait_ge(transposed, groups_before(t, n) + 1)
            src = turned[n % 2][:, 0:many * P].rearrange("d (n p) -> d n p", n=many)
            if first == 0:
                copy(dense_t[:, t, :], src[:, 0, :])
            copy(vecs[:, t, :, first:first + many].rearrange("d p n -> d n p"), src).then_inc(placed[n % 2], 1)

        def gram_cells(h, q, first, many):
            return gram[h][Q * q:Q * q + Q, 0:HALF * N].rearrange("k (p c) -> k c p", c=N)[:, first:first + many, :]

        def dot_cells(h, q, g, first, many):
            return pair_dots[Q * g:Q * g + Q, first:first + many, Q * q + HALF * h:Q * q + HALF * h + HALF]

        @block.vector
        def _(dve):
            dve.memset(one[:, :], 1.0).then_inc(one_made, 1)
            dve.memset(gram[0][:, 0:HALF * N], 0.0).then_inc(grams_cleared, 1)
            dve.wait_ge(ident_made, 1)
            dve.tensor_copy(ident16[:, :], ident[:, :]).then_inc(ident16_made, 1)
            dve.memset(gram[1][:, 0:HALF * N], 0.0).then_inc(grams_cleared, 1)
            dve.wait_ge(row_int_made, 2)
            dve.tensor_copy(row[:, :, :], row_int[:, :, :]).then_inc(row_made, 1)
            dve.tensor_scalar(minus_row[:, :, :], row_int[:, :, :], -1.0, None, ALU.mult).then_inc(minus_row_made, 1)
            dve.wait_ge(ids_loaded, 16)
            for m, f in enumerate(found):
                dve.tensor_copy(ids16[:, :, m], ids_sb[:, :, f]).then_inc(ids16_made, 1)
            dve.wait_ge(row_made, 1)
            for m in range(len(found)):
                if m >= 2:
                    dve.wait_ge(rows_picked, m - 1)
                for n, columns in enumerate(parts(m)):
                    dve.wait_ge(high_made, parts_through(m - 1) + n + 1)
                    dve.tensor_tensor(low[:, m % 2, columns], table[:, m % 2, columns], high[:, m % 2, columns],
                                      ALU.subtract).then_inc(low_made, 1)
                    for c in range(columns.start // P, min(columns.stop // P, CHUNKS[m] - 1)):
                        dve.wait_ge(wanted_made, m + 1)
                        dve.tensor_scalar(chunk_rows(m, c), wanted[0:height, m % 2, 0:width[m]],
                                          row[0:height, int(m >= len(FOUND)), c:c + 1], None,
                                          ALU.is_equal).then_inc(onehot_made, 1)
            dve.wait_ge(w1_dense_loaded, 32)
            dve.tensor_tensor(w_dense[:, :], w_dense[:, :], w_again[:, :], ALU.add).then_inc(weights_summed, 1)
            dve.wait_ge(weights_loaded, WEIGHTS * 16)

            def place_mine(t, groups):
                for n in groups:
                    if n % 2 == 0:
                        place(dve, dve.tensor_copy, t, n)

            place_mine(1, AFTER_PICKS)

            def lay_over(t):
                for h in range(2):
                    for q in range(NQ):
                        dve.wait_ge(laid_under, (t * 2 + h) * NQ + q + 1)
                        for g in range(NQ):
                            j, w = int(g == 0), quadrant_slots(g)
                            rows_over = over[Q * g:Q * g + Q, j:w].rearrange("k (j o) -> k j o", o=1)
                            last = dve.copy_predicated(dot_cells(h, q, g, j, w - j),
                                                       rows_over.to_broadcast([Q, w - j, HALF]),
                                                       gram_cells(h, q, RUN * g + j - 1, w - j))
                    last.then_inc(laid_over_all, 1)

            def keep(t):
                dve.wait_ge(layer3_done, t + 1)
                dve.tensor_copy(y_sb[0:1, :, t], top[0][0:1, P:2 * P]).then_inc(y_kept, 1)

            dve.wait_ge(over_loaded, 16)
            for t in range(tiles):
                lay_over(t)
                if t + 1 < tiles:
                    place_mine(t + 1, AFTER_DENSE[t])
                if t:
                    keep(t - 1)
                if t + 1 < tiles:
                    place_mine(t + 1, sum(AFTER_BLOCK[t], []))
                dve.wait_ge(layer1_done, t * 2 + 2)
                for u in range(half, u1):
                    last = dve.tensor_scalar(h1[:, u, :], acc[1][:, (u - half) * P:(u - half + 1) * P],
                                             b1_sb[:, u:u + 1], 0.0, ALU.add, ALU.max)
                last.then_inc(relu1[1], 1)
            keep(tiles - 1)

        @block.scalar
        def _(act):
            def copy(dst, src):
                return act.activation(dst, src, ACT.Copy)

            def place_picked(m):
                act.wait_ge(rows_picked, m + 1)
                v = found[m] + 1
                copy(vecs[:, first_tile[m]:, :, v].rearrange("d t p -> d (t p)"),
                     picked[m % 2][:, 0:width[m]]).then_inc(picked_placed, 1)
                for n in AFTER_PICK.get(m, []):
                    place(act, copy, 0, n)

            def split(m, n):
                if n < len(parts(m)) - 1:
                    act.wait_ge(first_half_loaded, 16)
                else:
                    act.wait_ge(table_loaded[m % 2], m // 2 * 16 + 16)
                if m >= 2:
                    act.wait_ge(rows_picked, m - 1)
                columns = parts(m)[n]
                copy(high[:, m % 2, columns], table[:, m % 2, columns]).then_inc(high_made, 1)

            for m in range(len(found)):
                split(m, 0)
                act.wait_ge(ids_sent, m + 1)
                if m >= 2:
                    act.wait_ge(onehot_made, vector_chunks_before(m - 1))
                copy(wanted[:, m % 2, 0:width[m]], sent_ids[m % 2][:, 0:width[m]]).then_inc(wanted_made, 1)
                for n in range(1, len(parts(m))):
                    split(m, n)
                act.wait_ge(minus_row_made, 1)
                act.wait_ge(one_made, 1)
                act.wait_ge(wanted_made, m + 1)
                last_chunk = CHUNKS[m] - 1
                act.activation(distance[:, 0:width[m]], wanted[0:height, m % 2, 0:width[m]], ACT.Abs,
                               bias=minus_row[0:height, int(m >= len(FOUND)), last_chunk:last_chunk + 1]
                               ).then_inc(distance_made, 1)
                act.wait_ge(distance_made, m + 1)
                act.activation(chunk_rows(m, last_chunk), distance[:, 0:width[m]], ACT.Relu, scale=-1.0,
                               bias=one[:, :]).then_inc(last_chunk_made, 1)
                if m >= 1:
                    place_picked(m - 1)
            act.wait_ge(weights_loaded, WEIGHTS * 16)

            def place_mine(t, groups):
                for n in groups:
                    if n % 2 == 1:
                        place(act, copy, t, n)

            place_mine(1, AFTER_PICKS)

            def lay_under(t):
                for h in range(2):
                    act.wait_ge(gram_done, t * 2 + h + 1)
                    for q in range(NQ):
                        for g in range(NQ):
                            w = quadrant_slots(g)
                            last = copy(dot_cells(h, q, g, 0, w), gram_cells(h, q, FOLD + RUN * g, w))
                        last.then_inc(laid_under, 1)

            def second_layer(t):
                for v in range(u2):
                    act.wait_ge(layer2_done, t * u2 + v + 1)
                    act.activation(h2[:, v, :], top[v][:, 0:P], ACT.Relu, bias=b2_sb[:, v:v + 1]).then_inc(relu2, 1)

            for t in range(tiles):
                lay_under(t)
                if t == 0:
                    place_picked(len(FOUND))
                if t:
                    second_layer(t - 1)
                if t + 1 < tiles:
                    place_mine(t + 1, AFTER_DENSE[t] + sum(AFTER_BLOCK[t][:half], []))
                act.wait_ge(layer1_done, t * 2 + 1)
                for u in range(half):
                    last = act.activation(h1[:, u, :], acc[0][:, u * P:(u + 1) * P], ACT.Relu,
                                          bias=b1_sb[:, u:u + 1])
                last.then_inc(relu1[0], 1)
                if t + 1 < tiles:
                    place_mine(t + 1, sum(AFTER_BLOCK[t][half:], []))
            second_layer(tiles - 1)

        @block.tensor
        def _(pe):
            def send_ids(m):
                if m >= 2:
                    pe.wait_ge(wanted_made, m - 1)
                pe.wait_ge(ids16_made, m + 1)
                for t in range(first_tile[m], tiles):
                    i = t - first_tile[m]
                    last = pe.matmul(sent_ids[m % 2][:, i * P:(i + 1) * P],
                                     ids16[:, t, m:m + 1].to_broadcast([P, P]), ident16[:, :], start=True, stop=True)
                last.then_inc(ids_sent, 1)

            def pick(m):
                if m >= 2:
                    pe.wait_ge(picked_placed, m - 1)
                for c in range(CHUNKS[m]):
                    pe.wait_ge(low_made, parts_through(m - 1) + sum(p.start <= c * P for p in parts(m)))
                    if c < CHUNKS[m] - 1:
                        pe.wait_ge(onehot_made, vector_chunks_before(m) + c + 1)
                    else:
                        pe.wait_ge(last_chunk_made, m + 1)
                    for part in (high, low):
                        last = pe.matmul(picked[m % 2][:, 0:width[m]], part[:, m % 2, c * P:(c + 1) * P],
                                         chunk_rows(m, c), start=(c == 0 and part is high),
                                         stop=(c == CHUNKS[m] - 1 and part is low))
                last.then_inc(rows_picked, 1)

            def transposes(t, groups):
                for n in groups:
                    first, many = GROUPS[n]
                    if t or n >= 2:
                        pe.wait_ge(placed[n % 2], groups_before(t, n, n % 2))
                    for v in range(first, first + many):
                        if v == 0:
                            pe.wait_ge(dense_loaded, 16)
                            src = dense_sb[:, t, :]
                        else:
                            pe.wait_ge(gathered[v - 1], 16 * (t + 1))
                            src = rows[:, t, GATHERED.index(v - 1), :]
                        last = pe.transpose(turned[n % 2][:, (v - first) * P:(v - first + 1) * P], src, ident[:, :])
                    last.then_inc(transposed, 1)

            def grams(t, h):
                if h == 0:
                    pe.wait_ge(picked_placed, len(FOUND) + int(t >= first_tile[-1]))
                    for b in range(2):
                        pe.wait_ge(placed[b], groups_before(t + 1, 0, b))
                    if t:
                        pe.wait_ge(laid_over_all, t * 2)
                for m in range(HALF):
                    for q in range(NQ):
                        p = Q * q + HALF * h + m
                        last = pe.matmul(gram[h][Q * q:Q * q + N, m * N:(m + 1) * N],
                                         vecs[:, t, p, :], vecs[:, t, p, :], start=True, stop=True)
                last.then_inc(gram_done, 1)

            def dense_products(t):
                for u in range(u1):
                    pe.matmul(acc[u // half][:, u % half * P:(u % half + 1) * P], w_dense[:, u * P:(u + 1) * P],
                              dense_t[:, t, :], start=(u % half == 0), stop=False, skip_group_check=True)

            def pair_products(t):
                pe.wait_ge(laid_over_all, t * 2 + 2)
                for u in range(u1):
                    for j in range(RUN):
                        k = Q * sum(j < quadrant_slots(g) for g in range(NQ))
                        last = pe.matmul(acc[u // half][:, u % half * P:(u % half + 1) * P],
                                         w_pair[0:k, j, u * P:(u + 1) * P], pair_dots[0:k, j, :],
                                         start=False, stop=(j == RUN - 1), skip_group_check=True)
                    if u % half == half - 1:
                        last.then_inc(layer1_done, 1)
                    if t + 1 < tiles:
                        transposes(t + 1, AFTER_BLOCK[t][u])

            def second_layer(t, e):
                if t and e == 0:
                    pe.wait_ge(y_kept, t)
                pe.wait_ge(relu1[e], t + 1)
                for v in range(u2):
                    for u in range(e * half, (e + 1) * half):
                        last = pe.matmul(top[v][:, 0:P], w2_sb[:, u, v * P:(v + 1) * P], h1[:, u, :],
                                         start=(u == 0), stop=(u == u1 - 1))
                    if e == 1:
                        last.then_inc(layer2_done, 1)

            def third_layer(t):
                for v in range(u2):
                    pe.wait_ge(relu2, t * u2 + v + 1)
                    last = pe.matmul(top[0][0:1, P:2 * P], w3_sb[:, v:v + 1], h2[:, v, :],
                                     start=(v == 0), stop=(v == u2 - 1))
                last.then_inc(layer3_done, 1)

            def warm_up(products):
                for _ in range(products):
                    pe.matmul(turned[0][:, 0:P], ident16[:, :], ident16[:, :], start=True, stop=True)

            pe.wait_ge(ident16_made, 1)
            warm_up(WARM_UP[0])
            send_ids(0)
            warm_up(WARM_UP[1])
            for m in range(len(FOUND)):
                send_ids(m + 1)
                pick(m)
                transposes(0, AFTER_PICK.get(m, []))
            transposes(1, AFTER_PICKS)
            pe.wait_ge(grams_cleared, 2)
            for t in range(tiles):
                grams(t, 0)
                if 0 < t < tiles - 1:
                    second_layer(t - 1, 0)
                grams(t, 1)
                if t == tiles - 1:
                    second_layer(t - 1, 0)
                if t:
                    second_layer(t - 1, 1)
                if t == 0:
                    pe.wait_ge(weights_summed, 1)
                    pe.wait_ge(weights_loaded, WEIGHTS * 16)
                    pick(len(FOUND))
                dense_products(t)
                if t + 1 < tiles:
                    transposes(t + 1, AFTER_DENSE[t])
                if t:
                    third_layer(t - 1)
                pair_products(t)
            for e in range(2):
                second_layer(tiles - 1, e)
            third_layer(tiles - 1)


def kernel(**inputs):
    import numpy as _np
    import concourse.bacc as _bacc
    from concourse.bass_utils import run_bass_kernel_spmd as _run

    nc = _bacc.Bacc("TRN2", target_bir_lowering=False, num_devices=1)
    arrays, args = {}, {}
    for name in inputs:
        a = _np.ascontiguousarray(inputs[name])
        arrays[f"in_{name}_dram"] = a
        args[name] = nc.dram_tensor(f"in_{name}_dram", a.shape, mybir.dt.from_np(a.dtype),
                                    kind="ExternalInput").ap()
    batch = inputs["r_dense_features"].shape[0]
    w1 = inputs["W_top1"]
    pair_weights = _np.zeros((P, RUN, w1.shape[1]), w1.dtype)
    over_rows = _np.zeros((P, RUN), _np.int32)
    for s in range(SLOTS):
        g, j = s // RUN, s % RUN
        for row in range(N):
            over_rows[Q * g + row, j] = laid_over(row, s)
            if pair_row(row, s) is not None:
                pair_weights[Q * g + row, j] = w1[P + pair_row(row, s)]
    for name, a in (("pair_weights", pair_weights), ("over_rows", over_rows)):
        arrays[name] = a
        args[name] = nc.dram_tensor(name, a.shape, mybir.dt.from_np(a.dtype), kind="ExternalInput").ap()
    out = nc.dram_tensor("out_dram", (batch, 1), F32, kind="ExternalOutput").ap()
    dlrm(nc, args["r_dense_features"], args["ids"], [args[f"tbl_{f}"] for f in range(FIELDS)], args["W_top1"],
         args["pair_weights"], args["over_rows"], args["b_top1"], args["W_top2"], args["b_top2"], args["W_top3"], out)
    r = _run(nc, [arrays], core_ids=[0])
    return r.results[0]["out_dram"]
```
